# Optimizing a Trainium2 kernel written in Bass

```python
import numpy as np
import jax
import jax.numpy as jnp

def _softmax(x, axis=-1):
    return jax.nn.softmax(x, axis=axis)

def _gelu(x):
    return jax.nn.gelu(x, approximate=True)

def _silu(x):
    return jax.nn.silu(x)

def _sigmoid(x):
    return jax.nn.sigmoid(x)

def _layernorm(x, axis=-1, eps=1e-05):
    m = jnp.mean(x, axis=axis, keepdims=True)
    v = jnp.var(x, axis=axis, keepdims=True)
    return (x - m) / jnp.sqrt(v + eps)

def _scatter_add(tgt, idx, src, axis=0):
    return tgt.at[idx].add(src)

def _segment_sum(src, seg, n):
    return jax.ops.segment_sum(src, seg, n)
kernel_name = 'mk_dlrm_tower_d1_rec_r8_147a77'

def setup_inputs(seed: int=0):
    np.random.seed(seed)
    _w = jnp.asarray

    def _rec_inputs():
        import jax
        import jax.numpy as jnp
        _tk = jax.random.key(seed)
        dense_ctx = jax.random.normal(jax.random.fold_in(_tk, 190), (512, 16), jnp.float32)
        ids = jnp.stack([jax.random.randint(jax.random.fold_in(_tk, 200 + f), (512,), 0, v, jnp.int32) for f, v in enumerate([1250, 1250, 12500, 1000, 12500, 1250, 12500, 1000, 1250, 1250, 1250, 12500, 12500, 1250, 12500, 12500])], axis=1)
        tbl_0 = 0.05 * jax.random.normal(jax.random.fold_in(_tk, 500 + 0), (1250, 256), jnp.float32)
        tbl_1 = 0.05 * jax.random.normal(jax.random.fold_in(_tk, 500 + 1), (1250, 256), jnp.float32)
        tbl_2 = 0.05 * jax.random.normal(jax.random.fold_in(_tk, 500 + 2), (12500, 256), jnp.float32)
        tbl_3 = 0.05 * jax.random.normal(jax.random.fold_in(_tk, 500 + 3), (1000, 256), jnp.float32)
        tbl_4 = 0.05 * jax.random.normal(jax.random.fold_in(_tk, 500 + 4), (12500, 256), jnp.float32)
        tbl_5 = 0.05 * jax.random.normal(jax.random.fold_in(_tk, 500 + 5), (1250, 256), jnp.float32)
        tbl_6 = 0.05 * jax.random.normal(jax.random.fold_in(_tk, 500 + 6), (12500, 256), jnp.float32)
        tbl_7 = 0.05 * jax.random.normal(jax.random.fold_in(_tk, 500 + 7), (1000, 256), jnp.float32)
        tbl_8 = 0.05 * jax.random.normal(jax.random.fold_in(_tk, 500 + 8), (1250, 256), jnp.float32)
        tbl_9 = 0.05 * jax.random.normal(jax.random.fold_in(_tk, 500 + 9), (1250, 256), jnp.float32)
        tbl_10 = 0.05 * jax.random.normal(jax.random.fold_in(_tk, 500 + 10), (1250, 256), jnp.float32)
        tbl_11 = 0.05 * jax.random.normal(jax.random.fold_in(_tk, 500 + 11), (12500, 256), jnp.float32)
        tbl_12 = 0.05 * jax.random.normal(jax.random.fold_in(_tk, 500 + 12), (12500, 256), jnp.float32)
        tbl_13 = 0.05 * jax.random.normal(jax.random.fold_in(_tk, 500 + 13), (1250, 256), jnp.float32)
        tbl_14 = 0.05 * jax.random.normal(jax.random.fold_in(_tk, 500 + 14), (12500, 256), jnp.float32)
        tbl_15 = 0.05 * jax.random.normal(jax.random.fold_in(_tk, 500 + 15), (12500, 256), jnp.float32)
        _rk = jax.random.fold_in(_tk, 7)
        W_top1 = 0.125 * jax.random.normal(jax.random.fold_in(_tk, 801), (64, 512), jnp.float32)
        W_top2 = 0.0441942 * jax.random.normal(jax.random.fold_in(_tk, 802), (512, 256), jnp.float32)
        W_top3 = 0.0625 * jax.random.normal(jax.random.fold_in(_tk, 803), (256, 1), jnp.float32)
        b_top1 = jnp.zeros((512,), jnp.float32)
        b_top2 = jnp.zeros((256,), jnp.float32)
        return (dense_ctx, ids, tbl_0, tbl_1, tbl_2, tbl_3, tbl_4, tbl_5, tbl_6, tbl_7, tbl_8, tbl_9, tbl_10, tbl_11, tbl_12, tbl_13, tbl_14, tbl_15, W_top1, b_top1, W_top2, b_top2, W_top3)
    dense_ctx, ids, tbl_0, tbl_1, tbl_2, tbl_3, tbl_4, tbl_5, tbl_6, tbl_7, tbl_8, tbl_9, tbl_10, tbl_11, tbl_12, tbl_13, tbl_14, tbl_15, W_top1, b_top1, W_top2, b_top2, W_top3 = _rec_inputs()

    def _L0_rec_setup():
        import jax, jax.numpy as jnp
        import numpy as np
        B, F, E = (512, 16, 256)
        N_LAYERS = 3
        key = jax.random.key(seed)
        k1, k2, k3 = jax.random.split(key, 3)
        x = jax.random.normal(k1, (B, F, E), dtype=jnp.float32)
        Ws = jax.random.normal(k2, (N_LAYERS, F, F * F), dtype=jnp.float32) * 0.05
        bs = jax.random.normal(k3, (N_LAYERS, F), dtype=jnp.float32) * 0.05
        return {'x': x, 'Ws': Ws, 'bs': bs}
    _L0_rec_all = _L0_rec_setup()
    _L0_rec_in = {k: v for k, v in _L0_rec_all.items() if k in ('Ws', 'bs')}
    del _L0_rec_all
    return {'dense_ctx': dense_ctx, 'ids': ids, 'tbl_0': tbl_0, 'tbl_1': tbl_1, 'tbl_2': tbl_2, 'tbl_3': tbl_3, 'tbl_4': tbl_4, 'tbl_5': tbl_5, 'tbl_6': tbl_6, 'tbl_7': tbl_7, 'tbl_8': tbl_8, 'tbl_9': tbl_9, 'tbl_10': tbl_10, 'tbl_11': tbl_11, 'tbl_12': tbl_12, 'tbl_13': tbl_13, 'tbl_14': tbl_14, 'tbl_15': tbl_15, 'W_top1': W_top1, 'b_top1': b_top1, 'W_top2': W_top2, 'b_top2': b_top2, 'W_top3': W_top3, 'L0_rec_Ws': _L0_rec_in['Ws'], 'L0_rec_bs': _L0_rec_in['bs']}

def reference(dense_ctx, ids, tbl_0, tbl_1, tbl_2, tbl_3, tbl_4, tbl_5, tbl_6, tbl_7, tbl_8, tbl_9, tbl_10, tbl_11, tbl_12, tbl_13, tbl_14, tbl_15, W_top1, b_top1, W_top2, b_top2, W_top3, L0_rec_Ws, L0_rec_bs):
    import jax
    import jax.numpy as jnp

    def _L0_rec_ref(x, Ws, bs):
        import jax, jax.numpy as jnp
        import numpy as np
        B, F, E = (512, 16, 256)
        N_LAYERS = 3
        B_, F_, E_ = x.shape
        n_layers = Ws.shape[0]
        xk = x
        outs = []
        for i in range(n_layers):
            z = jnp.einsum('bfe,bge->bfge', x, xk).reshape(B_, F_ * F_, E_)
            z = jnp.swapaxes(z, 1, 2)
            z = jnp.einsum('bcl,oc->bol', z, Ws[i]) + bs[i][None, :, None]
            z = jax.nn.relu(z)
            z = jnp.sum(z, axis=-1)
            outs.append(z)
            xk = jnp.broadcast_to(z[:, :, None], (B_, F_, E_))
        return jnp.concatenate(outs, axis=1)
    e = jnp.stack([tbl_0[ids[:, 0]], tbl_1[ids[:, 1]], tbl_2[ids[:, 2]], tbl_3[ids[:, 3]], tbl_4[ids[:, 4]], tbl_5[ids[:, 5]], tbl_6[ids[:, 6]], tbl_7[ids[:, 7]], tbl_8[ids[:, 8]], tbl_9[ids[:, 9]], tbl_10[ids[:, 10]], tbl_11[ids[:, 11]], tbl_12[ids[:, 12]], tbl_13[ids[:, 13]], tbl_14[ids[:, 14]], tbl_15[ids[:, 15]]], axis=1)
    z = _L0_rec_ref(e, L0_rec_Ws, L0_rec_bs)
    z = z.reshape(z.shape[0], -1)
    h = jnp.concatenate([z, dense_ctx], axis=1)
    h = jnp.maximum(h @ W_top1 + b_top1, 0.0)
    h = jnp.maximum(h @ W_top2 + b_top2, 0.0)
    y = h @ W_top3
    return y

_drawn_inputs = setup_inputs


def setup_inputs(seed=0):
    import zlib

    import numpy as np

    out = dict(_drawn_inputs(seed))
    spreads = {'b_top1': (0.0, 2.0), 'b_top2': (0.0, 2.0)}
    factors = {'dense_ctx': 8.0}
    for name, (base, spread) in spreads.items():
        noise = np.random.default_rng([zlib.crc32(name.encode()), seed]).standard_normal(out[name].shape)
        drawn = base * np.exp(spread * noise) if base else spread * noise
        out[name] = jnp.asarray(drawn.astype(out[name].dtype))
    for name, factor in factors.items():
        out[name] = (out[name] * factor).astype(out[name].dtype)
    return out
```

```python
from contextlib import ExitStack

import numpy as np

import concourse.bass as bass
from concourse import mybir

F32 = mybir.dt.float32
I32 = mybir.dt.int32
ACT = mybir.ActivationFunctionType
ALU = mybir.AluOpType
AX = mybir.AxisListType

B, F, E = 512, 16, 256
P = 128
GB = P // F
NT = 4
TR = P // NT
UB = NT * GB
UC = UB * F
NU = B // UB
NB = NU // 2
BT = 2 * GB
EC = E // P
PAIRS = F * (F - 1) // 2
QB = GB // 2
YC = QB * PAIRS
NS = NB + 1
H1, H2 = 512, 256
VOCAB = [1250, 1250, 12500, 1000, 12500, 1250, 12500, 1000, 1250, 1250, 1250, 12500, 12500, 1250,
         12500, 12500]
FIRST_PAIR = [0] + [sum(F - k for k in range(1, d)) for d in range(1, F)]
POOL_D = [1, 2]
DVE_D = [d for d in range(1, F) if d not in POOL_D]
MID = 6


def build(nc, table, ids, vocab, ident, mask_g, mask_j, spread0, spread1, sel, w0, w1a, w2a, bias,
          w1, b1, w2, b2, w3, dense, out):
    ctx = ExitStack()
    with ctx:
        def sb(name, shape, dt=F32):
            return ctx.enter_context(nc.sbuf_tensor(name, shape, dt))

        def pb(name, shape):
            return ctx.enter_context(nc.psum_tensor(name, shape, F32))

        def sem(name):
            return ctx.enter_context(nc.semaphore(name))

        ids_sb = sb("ids_sb", [P, B // GB], I32)
        vocab_sb = sb("vocab_sb", [P, 3])
        idf = sb("idf", [P, B // GB])
        idneg = sb("idneg", [P, B // GB])
        idx = sb("idx", [P, B // GB], I32)
        X = [sb(f"X{p}", [P, 2 * NT, E]) for p in range(2)]
        XT = [sb(f"XT{p}", [P, 2, EC, UC]) for p in range(2)]
        XX = sb("XX", [P, 2, EC, UC])
        PR = sb("PR", [P, 2, EC, UB, PAIRS])
        U = sb("U", [P, NS, BT, F])
        relu_d = sb("relu_d", [P, NB, BT, F])
        z_off = sb("z_off", [P, NB * BT])
        z_diag = sb("z_diag", [P, BT])
        z0 = sb("z0", [P, NB * BT])
        zl = sb("zl", [P, NS + 1, BT])
        zx = [sb(f"zx{k}", [P, BT, F]) for k in range(2)]
        prod = sb("prod", [P, BT, F, F])
        ident_sb = sb("ident_sb", [P, P])
        mask_g_sb = sb("mask_g_sb", [P, F])
        mask_j_sb = sb("mask_j_sb", [P, NT])
        spread_sb = [sb(f"spread{k}_sb", [P, P]) for k in range(2)]
        sel_sb = sb("sel_sb", [P, 3, 80])
        w0_sb = sb("w0_sb", [P, EC, TR])
        w1a_sb = sb("w1a_sb", [P, EC, TR])
        w2a_sb = sb("w2a_sb", [P, EC, TR])
        bias_sb = sb("bias_sb", [P, 2])
        bias2 = sb("bias2", [P, 1])
        w1_sb = sb("w1_sb", [P, H1])
        b1_sb = sb("b1_sb", [P, H1 // P])
        w2_sb = sb("w2_sb", [P, H1 // P, H2])
        b2_sb = sb("b2_sb", [P, H2 // P])
        w3_sb = sb("w3_sb", [P, H2 // P])
        zj = sb("zj", [P, 3, B])
        H = sb("H", [P, B])
        h1 = sb("h1", [P, H1 // P, B])
        h2 = sb("h2", [P, H2 // P, B])
        y_sb = sb("y_sb", [1, B])

        T = pb("T", [P, EC, UC])
        Y = pb("Y", [P, 4, 512])
        YD = pb("YD", [P, 512])
        ZB = pb("ZB", [P, BT, F * 2])

        ids_in = sem("ids_in")
        consts_in = sem("consts_in")
        weights_in = sem("weights_in")
        dense_in = sem("dense_in")
        index_ready = sem("index_ready")
        dve_step = sem("dve_step")
        bias2_ready = sem("bias2_ready")
        gathered = [sem("gathered_even"), sem("gathered_odd")]
        transposed = sem("transposed")
        xt_ready = sem("xt_ready")
        xx_ready = sem("xx_ready")
        dve_products = sem("dve_products")
        pool_products = sem("pool_products")
        yd_ready = sem("yd_ready")
        yd_read = sem("yd_read")
        y_ready = sem("y_ready")
        y_summed = sem("y_summed")
        z_diag_ready = sem("z_diag_ready")
        z0_ready = sem("z0_ready")
        zx_ready = sem("zx_ready")
        zb_ready = sem("zb_ready")
        prod_ready = sem("prod_ready")
        stage_summed = sem("stage_summed")
        zj_ready = sem("zj_ready")
        h_cleared = sem("h_cleared")
        h_psum = sem("h_psum")
        h_ready = sem("h_ready")
        h1_ready = sem("h1_ready")
        h1_relu = sem("h1_relu")
        h2_ready = sem("h2_ready")
        h2_relu = sem("h2_relu")
        out_ready = sem("out_ready")
        y_copied = sem("y_copied")
        stored = sem("stored")

        def wait(eng, s, value):
            if not isinstance(value, int) or value > 0:
                eng.wait_ge(s, value)

        def slots(engine, body):
            for p in range(2):
                body(0, p, False, False)
            with engine.Fori(1, NB // 2 - 1) as i:
                for p in range(2):
                    body(i, p, True, False)
            for p in range(2):
                body(NB // 2 - 1, p, True, p == 1)

        block = ctx.enter_context(nc.Block())

        @block.sync
        def _(sp):
            sp.dma_start(ids_sb[:], ids).then_inc(ids_in, 16)
            sp.dma_start(vocab_sb[:], vocab).then_inc(ids_in, 16)
            for tile, src in ((ident_sb, ident), (w0_sb, w0), (w1a_sb, w1a), (w2a_sb, w2a),
                              (bias_sb, bias), (mask_g_sb, mask_g), (mask_j_sb, mask_j),
                              (spread_sb[0], spread0), (spread_sb[1], spread1)):
                sp.dma_start(tile[:], src).then_inc(consts_in, 16)
            for tile, src in ((sel_sb, sel), (w1_sb, w1), (b1_sb, b1), (w2_sb, w2), (b2_sb, b2),
                              (w3_sb, w3)):
                sp.dma_start(tile[:], src).then_inc(weights_in, 16)
            sp.wait_ge(h_cleared, 1)
            sp.dma_start(H[96:96 + F, :], dense).then_inc(dense_in, 16)
            sp.wait_ge(y_copied, 1)
            sp.dma_start(out, y_sb[:]).then_inc(stored, 16)
            sp.wait_ge(stored, 16)

        def multiply(eng, p, u, d):
            n = F - d
            x = XT[p][:, u, :, :].rearrange("q c (b f) -> q (c b) f", f=F)
            o = PR[:, u, :, :, :].rearrange("q c b s -> q (c b) s")
            return eng.tensor_tensor(o[:, :, FIRST_PAIR[d]:FIRST_PAIR[d] + n], x[:, :, 0:n],
                                     x[:, :, d:F], ALU.mult)

        @block.gpsimd
        def _(pool):
            pool.wait_ge(index_ready, 1)

            def gather(t):
                wait(pool, transposed, 2 * (t - 1))
                wait(pool, gathered[t % 2], 16 * 2 * NT * (t // 2))
                for g in range(2 * NT):
                    pool.indirect_dma_start(
                        out=X[t % 2][:, g, :], out_offset=None, in_=table,
                        in_offset=bass.IndirectOffsetOnAxis(
                            ap=idx[:, 2 * NT * t + g:2 * NT * t + g + 1], axis=0),
                    ).then_inc(gathered[t % 2], 16)

            gather(0)
            gather(1)
            for t in range(NB):
                for u in range(2):
                    n = 2 * t + u
                    pool.wait_ge(xt_ready, n + 1)
                    wait(pool, y_ready, n - 1)
                    for d in POOL_D:
                        last = multiply(pool, t % 2, u, d)
                    last.then_inc(pool_products, 1)
                if t + 2 < NB:
                    gather(t + 2)

        @block.scalar
        def _(act):
            def fill(i, p, u):
                n = 4 * i + 2 * p + u
                act.wait_ge(transposed, n + 1)
                if u == 0:
                    wait(act, dve_products, n - 2)
                    wait(act, pool_products, n - 2)
                    wait(act, yd_ready, n)
                act.activation(XT[p][:, u, :, :], T[:], ACT.Copy).then_inc(xt_ready, 1)
                wait(act, yd_ready, n - 1)
                act.activation(XX[:, u, :, :], T[:], ACT.Square).then_inc(xx_ready, 1)

            def read_yd(n, t, u):
                act.wait_ge(yd_ready, n + 1)
                act.activation(relu_d[:, bass.ds(t, 1), u * GB:(u + 1) * GB, :], YD[:, 0:P],
                               ACT.Relu, bias=bias_sb[:, 0:1]).then_inc(yd_read, 1)
                act.activation(U[:, bass.ds(t, 1), u * GB:(u + 1) * GB, :], YD[:, P:2 * P],
                               ACT.Copy).then_inc(yd_read, 1)

            def sum_y(n, u):
                act.wait_ge(y_ready, n + 1)
                for r in range(2):
                    for b in range(QB):
                        y = Y[:, 2 * u + r, b * PAIRS:(b + 1) * PAIRS]
                        last = act.activation(y, y, ACT.Relu, bias=bias2[:], scale=2.0,
                                              accum_out=z_off[:, bass.ds(n * GB + r * QB + b, 1)])
                last.then_inc(y_summed, 1)

            def sum_stage(s):
                act.wait_ge(prod_ready, s + 1)
                for b in range(BT):
                    q = prod[:, b, :, :]
                    last = act.activation(q, q, ACT.Relu, bias=bias_sb[:, 1:2],
                                          accum_out=zl[:, bass.ds(s + 1, 1), b:b + 1])
                last.then_inc(stage_summed, 1)

            fill(0, 0, 0)
            act.wait_ge(consts_in, 16 * 9)
            act.wait_ge(bias2_ready, 1)

            def slot(i, p, staged, last):
                t = 2 * i + p
                fill(i, p, 1)
                read_yd(2 * t, t, 0)
                if staged or p:
                    sum_y(2 * t - 1, 1)
                if not last:
                    fill(i + p, 1 - p, 0)
                read_yd(2 * t + 1, t, 1)
                if staged:
                    sum_stage(t - 2)
                sum_y(2 * t, 0)

            slots(nc.scalar, slot)
            sum_y(NU - 1, 1)
            act.wait_ge(yd_ready, NU + 1)
            act.activation(U[:, NB, :, :], YD[:, 0:2 * P], ACT.Copy).then_inc(yd_read, 1)
            for s in range(NS - 3, NS):
                sum_stage(s)

            act.wait_ge(weights_in, 16 * 6)
            for c in range(H1 // P):
                act.wait_ge(h1_ready, c + 1)
                act.activation(h1[:, c, :], Y[:, c, :], ACT.Relu, bias=b1_sb[:, c:c + 1])\
                    .then_inc(h1_relu, 1)
            for c in range(H2 // P):
                act.wait_ge(h2_ready, c + 1)
                act.activation(h2[:, c, :], T[:, c, :], ACT.Relu, bias=b2_sb[:, c:c + 1])\
                    .then_inc(h2_relu, 1)
            act.wait_ge(out_ready, 1)
            act.activation(y_sb[:], YD[0:1, :], ACT.Copy).then_inc(y_copied, 1)

        @block.vector
        def _(dve):
            chain = [0]

            def link(ins):
                chain[0] += 1
                ins.then_inc(dve_step, 1)
                dve.wait_ge(dve_step, chain[0])

            dve.wait_ge(ids_in, 32)
            link(dve.tensor_scalar(idneg[:], ids_sb[:], 0.0, vocab_sb[:, 0:1], ALU.is_lt, ALU.mult))
            link(dve.tensor_tensor(idf[:], ids_sb[:], idneg[:], ALU.add))
            link(dve.tensor_scalar(idneg[:], idf[:], 0.0, vocab_sb[:, 1:2], ALU.max, ALU.min))
            dve.tensor_scalar(idx[:], idneg[:], vocab_sb[:, 2:3], None, ALU.add)\
                .then_inc(index_ready, 1)
            dve.memset(H[:], 0.0).then_inc(h_cleared, 1)
            link(dve.memset(zl[:, 0, :], 0.0))
            dve.wait_ge(consts_in, 16 * 9)
            dve.tensor_scalar(bias2[:], bias_sb[:, 0:1], 2.0, None, ALU.mult)\
                .then_inc(bias2_ready, 1)

            def spread_z0(s):
                dve.wait_ge(y_summed, 2 * s + 2)
                dve.wait_ge(yd_read, 4 * s + 4)
                dve.tensor_reduce(z_diag[:], relu_d[:, bass.ds(s, 1), :, :], axis=AX.X, op=ALU.add)\
                    .then_inc(z_diag_ready, 1)
                dve.wait_ge(z_diag_ready, s + 1)
                dve.tensor_tensor(z0[:, bass.ds(s * BT, BT)], z_off[:, bass.ds(s * BT, BT)],
                                  z_diag[:], ALU.add).then_inc(z0_ready, 1)
                dve.wait_ge(z0_ready, s + 1)
                wait(dve, zb_ready, s)
                spread(zx[0], z0[:, bass.ds(s * BT, BT)].rearrange("q (b x) -> q b x", x=1))

            def spread_zl(s):
                wait(dve, stage_summed, s)
                spread(zx[1], zl[:, bass.ds(s, 1), :].rearrange("q x b -> q b x"))

            def spread(dst, src):
                dve.tensor_tensor(dst[:], src.broadcast_to([P, BT, F]),
                                  mask_g_sb[:].rearrange("q (x g) -> q x g", x=1)
                                  .broadcast_to([P, BT, F]), ALU.mult).then_inc(zx_ready, 1)

            def outer(s):
                dve.wait_ge(zb_ready, s + 1)
                wait(dve, stage_summed, s)
                dve.tensor_tensor(
                    prod[:],
                    U[:, bass.ds(s, 1), :, :].rearrange("q x b f -> q b f x")
                    .broadcast_to([P, BT, F, F]),
                    ZB[:, :, 0:F].rearrange("q b (x g) -> q b x g", x=1)
                    .broadcast_to([P, BT, F, F]), ALU.mult).then_inc(prod_ready, 1)

            def products(n, p, u, distances):
                for d in distances:
                    last = multiply(dve, p, u, d)
                return last

            def spread_all(l):
                if l == 0:
                    dve.wait_ge(z0_ready, NB)
                    src = z0[:]
                else:
                    dve.wait_ge(stage_summed, NB - 1 + l)
                    src = zl[:, l:l + NB, :].rearrange("q s b -> q (s b)")
                dve.tensor_tensor(
                    zj[:, l, :].rearrange("q (n j b) -> q n j b", n=NU, j=NT),
                    src.rearrange("q (n x b) -> q n x b", n=NU, x=1).broadcast_to([P, NU, NT, GB]),
                    mask_j_sb[:].rearrange("q (x j y) -> q x j y", x=1, y=1)
                    .broadcast_to([P, NU, NT, GB]), ALU.mult).then_inc(zj_ready, 1)

            def slot(i, p, staged, last):
                t = 2 * i + p
                for u in range(2):
                    n = 2 * t + u
                    dve.wait_ge(xt_ready, n + 1)
                    wait(dve, y_ready, n - 1)
                    products(n, p, u, DVE_D[:MID])
                    if staged and u == 0:
                        spread_z0(t - 2)
                        spread_zl(t - 2)
                    products(n, p, u, DVE_D[MID:]).then_inc(dve_products, 1)
                    if staged and u == 0:
                        outer(t - 2)

            slots(nc.vector, slot)

            for s in range(NS - 3, NS):
                if s < NB:
                    spread_z0(s)
                if s == NB - 1:
                    spread_all(0)
                spread_zl(s)
                if s == NB:
                    dve.wait_ge(yd_read, 2 * NU + 1)
                outer(s)
            spread_all(1)
            spread_all(2)
            dve.wait_ge(dense_in, 16)
            dve.wait_ge(h_psum, 1)
            dve.tensor_copy(H[0:80, :], ZB[:].rearrange("q b f -> q (b f)")[0:80, :])\
                .then_inc(h_ready, 1)

        @block.tensor
        def _(pe):
            def transpose(i, p, u):
                n = 4 * i + 2 * p + u
                pe.wait_ge(gathered[p], 16 * 2 * NT * (i + 1))
                wait(pe, xt_ready, n)
                wait(pe, xx_ready, n)
                for c in range(EC):
                    for j in range(NT):
                        last = pe.transpose(T[:, c, j * P:(j + 1) * P],
                                            X[p][:, u * NT + j, c * P:(c + 1) * P], ident_sb[:])
                last.then_inc(transposed, 1)

            def small(cols, weights, src):
                terms = [(w, s, c) for w, s in zip(weights, src) for c in range(EC)]
                for k, (w, s, c) in enumerate(terms):
                    for j in range(NT):
                        last = pe.matmul(YD[TR * j:TR * j + TR, cols:cols + P], w[:, c, :],
                                         s[:, c, j * P:(j + 1) * P], start=k == 0,
                                         stop=k == len(terms) - 1)
                return last

            def squares_and_u(n, p, u, first):
                pe.wait_ge(xt_ready, n + 1)
                pe.wait_ge(xx_ready, n + 1)
                wait(pe, yd_read, 2 * n)
                small(0, [w0_sb], [XX[:, u, :, :]])
                ws, xs = ([w1a_sb], [XT[p][:, u, :, :]]) if first else \
                    ([w1a_sb, w2a_sb], [XT[p][:, u, :, :], XT[1 - p][:, u, :, :]])
                small(P, ws, xs).then_inc(yd_ready, 1)

            def contract(n, u):
                pe.wait_ge(dve_products, n + 1)
                pe.wait_ge(pool_products, n + 1)
                wait(pe, y_summed, n - 1)
                for r in range(2):
                    for c in range(EC):
                        for j in range(NT):
                            b = GB * j + QB * r
                            last = pe.matmul(
                                Y[TR * j:TR * j + TR, 2 * u + r, 0:YC], w0_sb[:, c, :],
                                PR[:, u, c, b:b + QB, :].rearrange("q b s -> q (b s)"),
                                start=c == 0, stop=c == EC - 1)
                last.then_inc(y_ready, 1)

            def spread_rows(s, layers):
                pe.wait_ge(zx_ready, 2 * s + len(layers))
                wait(pe, prod_ready, s)
                for k in layers:
                    last = pe.matmul(ZB[:, :, 0:F], spread_sb[k][:], zx[k][:],
                                     start=k == layers[0], stop=k == layers[-1])
                last.then_inc(zb_ready, 1)

            pe.wait_ge(consts_in, 16 * 9)
            transpose(0, 0, 0)

            def slot(i, p, staged, last):
                t = 2 * i + p
                transpose(i, p, 1)
                squares_and_u(2 * t, p, 0, not staged and p == 0)
                if staged:
                    spread_rows(t - 2, [0, 1])
                contract(2 * t, 0)
                if not last:
                    transpose(i + p, 1 - p, 0)
                squares_and_u(2 * t + 1, p, 1, not staged and p == 0)
                contract(2 * t + 1, 1)

            slots(nc.tensor, slot)
            wait(pe, yd_read, 2 * NU)
            for u in range(2):
                last = small(u * P, [w2a_sb], [XT[1][:, u, :, :]])
            last.then_inc(yd_ready, 1)
            for s in range(NS - 3, NB):
                spread_rows(s, [0, 1])
            spread_rows(NB, [1])

            pe.wait_ge(weights_in, 16 * 6)
            pe.wait_ge(zj_ready, 3)
            hp = ZB[:].rearrange("q b f -> q (b f)")[0:80, :]
            for l in range(3):
                last = pe.matmul(hp, sel_sb[:, l, :], zj[:, l, :], start=l == 0, stop=l == 2)
            last.then_inc(h_psum, 1)
            pe.wait_ge(h_ready, 1)
            for c in range(H1 // P):
                pe.matmul(Y[:, c, :], w1_sb[:, c * P:(c + 1) * P], H[:], start=True, stop=True)\
                    .then_inc(h1_ready, 1)
            for c in range(H2 // P):
                for k in range(H1 // P):
                    pe.wait_ge(h1_relu, k + 1)
                    last = pe.matmul(T[:, c, :], w2_sb[:, k, c * P:(c + 1) * P], h1[:, k, :],
                                     start=k == 0, stop=k == H1 // P - 1)
                last.then_inc(h2_ready, 1)
            for c in range(H2 // P):
                pe.wait_ge(h2_relu, c + 1)
                last = pe.matmul(YD[0:1, :], w3_sb[:, c:c + 1], h2[:, c, :], start=c == 0,
                                 stop=c == H2 // P - 1)
            last.then_inc(out_ready, 1)


def layout(inputs):
    f32 = np.float32
    a = {k: np.asarray(v) for k, v in inputs.items()}
    p = np.arange(P)
    first = np.concatenate([[0], np.cumsum(VOCAB)[:-1]])
    vocab = np.stack([np.tile(v, GB) for v in (np.array(VOCAB), np.array(VOCAB) - 1, first)],
                     axis=1).astype(f32)

    def halves(low, high):
        w = np.zeros((EC, P, TR), f32)
        for at, l in ((0, low), (F, high)):
            if l is not None:
                w[:, :, at:at + F] = a["L0_rec_Ws"][l].T.reshape(EC, P, F)
        return w.transpose(1, 0, 2)

    row, tile = p % TR, p // TR
    same = tile[:, None] == tile[None, :]
    low = row < F
    sel = np.zeros((P, 3, 80), f32)
    for l, rows in ((0, low), (1, low), (2, ~low)):
        sel[p[rows], l, 32 * l + row[rows] % F] = 1
    bs = a["L0_rec_bs"]
    w1 = np.zeros((P, H1), f32)
    for l in range(4):
        w1[32 * l:32 * l + F] = a["W_top1"][F * l:F * l + F]
    return {
        "table": np.concatenate([a[f"tbl_{f}"] for f in range(F)], axis=0),
        "ids": a["ids"].reshape(B // GB, P).T, "vocab": vocab,
        "ident": np.eye(P, dtype=f32),
        "mask_g": (row[:, None] % F == np.arange(F)).astype(f32),
        "mask_j": (tile[:, None] == np.arange(NT)).astype(f32),
        "spread0": (same & low[:, None] & low[None, :]).astype(f32),
        "spread1": (same & low[:, None] & ~low[None, :]).astype(f32),
        "sel": sel,
        "w0": halves(0, 0), "w1a": halves(1, None), "w2a": halves(None, 2),
        "bias": np.stack([np.tile(np.concatenate([bs[0], bs[0]]), NT),
                          np.tile(np.concatenate([bs[1], bs[2]]), NT)], axis=1),
        "w1": w1, "b1": a["b_top1"].reshape(H1 // P, P).T,
        "w2": a["W_top2"].reshape(H1 // P, P, H2).transpose(1, 0, 2),
        "b2": a["b_top2"].reshape(H2 // P, P).T,
        "w3": a["W_top3"].reshape(H2 // P, P).T,
        "dense": a["dense_ctx"].T,
    }


def kernel(**inputs):
    import concourse.bacc as bacc
    from concourse.bass_utils import run_bass_kernel_spmd

    nc = bacc.Bacc("TRN2", target_bir_lowering=False, num_devices=1)
    arrays, args = {}, {}
    for name, v in layout(inputs).items():
        v = np.ascontiguousarray(v)
        arrays[f"in_{name}"] = v
        args[name] = nc.dram_tensor(f"in_{name}", v.shape, mybir.dt.from_np(v.dtype),
                                    kind="ExternalInput").ap()
    out = nc.dram_tensor("out_0", (1, B), F32, kind="ExternalOutput").ap()
    build(nc, out=out, **args)
    r = run_bass_kernel_spmd(nc, [arrays], core_ids=[0])
    return r.results[0]["out_0"].reshape(B, 1)
```

```python
from contextlib import ExitStack

import numpy as np

import concourse.bass as bass
from concourse import mybir

F32 = mybir.dt.float32
I32 = mybir.dt.int32
ACT = mybir.ActivationFunctionType
ALU = mybir.AluOpType
AX = mybir.AxisListType

B, F, E = 512, 16, 256
P = 128
GB = P // F
NT = 4
TR = P // NT
UB = NT * GB
UC = UB * F
NU = B // UB
NV = 4
EC = E // P
PAIRS = F * (F - 1) // 2
QB = GB // 2
YC = QB * PAIRS
NS = NU + 1
H1, H2 = 512, 256
HC1, HC2 = H1 // P, H2 // P
VOCAB = [1250, 1250, 12500, 1000, 12500, 1250, 12500, 1000, 1250, 1250, 1250, 12500, 12500, 1250,
         12500, 12500]
FIRST_PAIR = [0] + [sum(F - k for k in range(1, d)) for d in range(1, F)]
POOL_D = [1, 2, 9]
POOL_ENDS = {0: [1, 9], 1: [1, 9], NU - 2: [1, 2, 3, 9, 10], NU - 1: [1, 2, 3, 4, 9]}
CUT1, CUT2 = 2, 6
ROWS = 80
MLP = [(0, 8), (8, 4), (12, 4)]
PER_MLP = 1 + HC1 + HC2 + 1


def pool_distances(n):
    return POOL_ENDS.get(n, POOL_D) if isinstance(n, int) else POOL_D


def dve_distances(n):
    return [d for d in range(1, F) if d not in pool_distances(n)]


def build(nc, table, ids, vocab, ident, mask_g, mask_j, spread0, spread1, sel, w0, w1a, w2a, bias,
          w1, b1, w2, b2, w3, dense, out):
    ctx = ExitStack()
    with ctx:
        def sb(name, shape, dt=F32):
            return ctx.enter_context(nc.sbuf_tensor(name, shape, dt))

        def pb(name, shape):
            return ctx.enter_context(nc.psum_tensor(name, shape, F32))

        def sem(name):
            return ctx.enter_context(nc.semaphore(name))

        ids_sb = sb("ids_sb", [P, B // GB], I32)
        vocab_sb = sb("vocab_sb", [P, 3])
        idf = sb("idf", [P, B // GB])
        idneg = sb("idneg", [P, B // GB])
        idx = sb("idx", [P, B // GB], I32)
        X = sb("X", [P, NV, NT, E])
        XT = sb("XT", [P, NV, EC, UC])
        XX = sb("XX", [P, 2, EC, UC])
        PR = sb("PR", [P, 2, EC, UB, PAIRS])
        U = sb("U", [P, NS, GB, F])
        relu_d = sb("relu_d", [P, NU, GB, F])
        z_off = sb("z_off", [P, NU * GB])
        z_diag = sb("z_diag", [P, GB])
        z0 = sb("z0", [P, NU * GB])
        zl = sb("zl", [P, NS + 1, GB])
        zx = [sb(f"zx{k}", [P, GB, F]) for k in range(2)]
        prod = sb("prod", [P, GB, F, F])
        zeros = sb("zeros", [P, F * F])
        ident_sb = sb("ident_sb", [P, P])
        mask_g_sb = sb("mask_g_sb", [P, F])
        mask_j_sb = sb("mask_j_sb", [P, NT])
        spread_sb = [sb(f"spread{k}_sb", [P, P]) for k in range(2)]
        sel_sb = sb("sel_sb", [P, 3, ROWS])
        w0_sb = sb("w0_sb", [P, EC, TR])
        w1a_sb = sb("w1a_sb", [P, EC, TR])
        w2a_sb = sb("w2a_sb", [P, EC, TR])
        bias_sb = sb("bias_sb", [P, 2])
        bias2 = sb("bias2", [P, 1])
        w1_sb = sb("w1_sb", [P, H1])
        b1_sb = sb("b1_sb", [P, HC1])
        w2_sb = sb("w2_sb", [P, HC1, H2])
        b2_sb = sb("b2_sb", [P, HC2])
        w3_sb = sb("w3_sb", [P, HC2])
        zj = sb("zj", [P, 3, B])
        H = sb("H", [P, B])
        h1 = sb("h1", [P, HC1, B])
        h2 = sb("h2", [P, HC2, B])
        y_sb = sb("y_sb", [1, B])

        T = pb("T", [P, EC, UC])
        Y = pb("Y", [P, 4, 512])
        YD = pb("YD", [P, 512])
        ZB = pb("ZB", [P, 512])
        zb = ZB[:, 0:GB * F].rearrange("q (b g) -> q b g", b=GB)

        ids_in = sem("ids_in")
        consts_in = sem("consts_in")
        weights_in = sem("weights_in")
        dense_in = sem("dense_in")
        index_ready = sem("index_ready")
        dve_step = sem("dve_step")
        bias2_ready = sem("bias2_ready")
        first_rows = [sem(f"first_rows{g}") for g in range(NT)]
        gathered = [sem(f"gathered{v}") for v in range(NV)]
        transposed = sem("transposed")
        xt_ready = sem("xt_ready")
        xx_ready = sem("xx_ready")
        dve_products = sem("dve_products")
        pool_products = sem("pool_products")
        yd_ready = sem("yd_ready")
        yd_read = sem("yd_read")
        y_ready = sem("y_ready")
        y_summed = sem("y_summed")
        z_diag_ready = sem("z_diag_ready")
        z0_ready = sem("z0_ready")
        zx_ready = sem("zx_ready")
        zb_ready = sem("zb_ready")
        prod_ready = sem("prod_ready")
        stage_summed = sem("stage_summed")
        tail_prod = sem("tail_prod")
        tail_act = sem("tail_act")
        tail_dve = sem("tail_dve")
        zj_ready = sem("zj_ready")
        h_cleared = sem("h_cleared")
        mlp_psum = sem("mlp_psum")
        mlp_sbuf = sem("mlp_sbuf")
        stored = sem("stored")

        def wait(eng, s, value):
            if not isinstance(value, int) or value > 0:
                eng.wait_ge(s, value)

        def steps(engine, body):
            for v in range(NV):
                body(0, v)
            with engine.Fori(1, NU // NV - 1) as i:
                for v in range(NV):
                    body(i, v)
            for v in range(NV):
                body(NU // NV - 1, v)

        def mlp_psum_tiles(k, phase):
            w = MLP[k][1] * UB
            flat = T[:].rearrange("q c n -> q (c n)")
            if k == 0 and phase < 2:
                return [flat[0:(ROWS, P)[phase], c * w:(c + 1) * w]
                        for c in range((1, HC1)[phase])], True
            if k == 1 and phase == 1:
                return [flat[:, c * w:(c + 1) * w] for c in range(HC1)], True
            if k == 1 and phase == 2:
                return [T[:, 1, c * w:(c + 1) * w] for c in range(HC2)], True
            if phase == 0:
                return [(None, Y[0:ROWS, 1, 0:w], ZB[0:ROWS, 0:w])[k]], False
            if phase == 1:
                return [Y[:, c, 0:w] for c in range(HC1)], False
            if phase == 2:
                return [T[:, c, 0:w] for c in range(HC2)], False
            return [(Y[0:1, 0, 0:w], Y[0:1, 0, 0:w], YD[0:1, 0:w])[k]], False

        def rows_of(v, i):
            return 16 * NT * (i + 1 - (v == 0))

        def before(n, limit):
            return not isinstance(n, int) or n < limit

        def after(n, limit):
            return not isinstance(n, int) or n >= limit

        block = ctx.enter_context(nc.Block())

        @block.sync
        def _(sp):
            sp.dma_start(ids_sb[:], ids).then_inc(ids_in, 16)
            sp.dma_start(vocab_sb[:], vocab).then_inc(ids_in, 16)
            for tile, src in ((ident_sb, ident), (w0_sb, w0), (w1a_sb, w1a), (w2a_sb, w2a),
                              (bias_sb, bias), (mask_g_sb, mask_g), (mask_j_sb, mask_j),
                              (spread_sb[0], spread0), (spread_sb[1], spread1)):
                sp.dma_start(tile[:], src).then_inc(consts_in, 16)
            for tile, src in ((sel_sb, sel), (w1_sb, w1), (b1_sb, b1), (w2_sb, w2), (b2_sb, b2),
                              (w3_sb, w3)):
                sp.dma_start(tile[:], src).then_inc(weights_in, 16)
            sp.wait_ge(h_cleared, 1)
            sp.dma_start(H[96:96 + F, :], dense).then_inc(dense_in, 16)
            sp.wait_ge(mlp_sbuf, PER_MLP * len(MLP))
            sp.dma_start(out, y_sb[:]).then_inc(stored, 16)
            sp.wait_ge(stored, 16)

        def multiply(eng, v, d):
            n = F - d
            x = XT[:, v, :, :].rearrange("q c (b f) -> q (c b) f", f=F)
            o = PR[:, v % 2, :, :, :].rearrange("q c b s -> q (c b) s")
            return eng.tensor_tensor(o[:, :, FIRST_PAIR[d]:FIRST_PAIR[d] + n], x[:, :, 0:n],
                                     x[:, :, d:F], ALU.mult)

        @block.gpsimd
        def _(pool):
            pool.wait_ge(index_ready, 1)

            def gather(n):
                wait(pool, transposed, n - NV + 1)
                wait(pool, gathered[n % NV], rows_of(n % NV, n // NV - 1))
                for g in range(NT):
                    pool.indirect_dma_start(
                        out=X[:, n % NV, g, :], out_offset=None, in_=table,
                        in_offset=bass.IndirectOffsetOnAxis(
                            ap=idx[:, NT * n + g:NT * n + g + 1], axis=0),
                    ).then_inc(gathered[n % NV] if n else first_rows[g], 16)

            gather(0)
            gather(1)
            gather(2)
            for n in range(NU):
                pool.wait_ge(xt_ready, n + 1)
                wait(pool, y_ready, 2 * (n - 1))
                for d in pool_distances(n):
                    last = multiply(pool, n % NV, d)
                last.then_inc(pool_products, 1)
                if 1 <= n < NU - 2:
                    gather(n + 2)

        @block.scalar
        def _(act):
            def fill(n, v):
                act.wait_ge(transposed, n + 1)
                wait(act, dve_products, n - NV + 1)
                wait(act, pool_products, n - NV + 1)
                wait(act, yd_ready, n - NV + 2)
                act.activation(XT[:, v, :, :], T[:], ACT.Copy).then_inc(xt_ready, 1)
                wait(act, yd_ready, n - 1)
                act.activation(XX[:, v % 2, :, :], T[:], ACT.Square).then_inc(xx_ready, 1)

            def read_yd(n):
                act.wait_ge(yd_ready, n + 1)
                act.activation(relu_d[:, bass.ds(n, 1), :, :], YD[:, 0:P], ACT.Relu,
                               bias=bias_sb[:, 0:1]).then_inc(yd_read, 1)
                act.activation(U[:, bass.ds(n, 1), :, :], YD[:, P:2 * P], ACT.Copy)\
                    .then_inc(yd_read, 1)

            def sum_y(n, parity):
                for r in range(2):
                    act.wait_ge(y_ready, 2 * n + r + 1)
                    for b in range(QB):
                        y = Y[:, 2 * parity + r, b * PAIRS:(b + 1) * PAIRS]
                        last = act.activation(y, y, ACT.Relu, bias=bias2[:], scale=2.0,
                                              accum_out=z_off[:, bass.ds(n * GB + r * QB + b, 1)])
                last.then_inc(y_summed, 1)

            def sum_prod(s, samples):
                for b in samples:
                    q = prod[:, b, :, :]
                    last = act.activation(q, q, ACT.Relu, bias=bias_sb[:, 1:2],
                                          accum_out=zl[:, bass.ds(s + 1, 1), b:b + 1])
                return last

            def mlp(k, phase):
                psum, whole = mlp_psum_tiles(k, phase)
                u0, nu = MLP[k]
                cols = slice(u0 * UB, (u0 + nu) * UB)
                first, size = ((0, 1), (1, HC1), (1 + HC1, HC2), (1 + HC1 + HC2, 1))[phase]
                for c in range(size):
                    done = PER_MLP * k + first + (size if whole else c + 1)
                    act.wait_ge(mlp_psum, done)
                    if phase == 0:
                        ins = act.activation(H[0:ROWS, cols], psum[c], ACT.Copy)
                    elif phase == 1:
                        ins = act.activation(h1[:, c, cols], psum[c], ACT.Relu,
                                             bias=b1_sb[:, c:c + 1])
                    elif phase == 2:
                        ins = act.activation(h2[:, c, cols], psum[c], ACT.Relu,
                                             bias=b2_sb[:, c:c + 1])
                    else:
                        ins = act.activation(y_sb[:, cols], psum[c], ACT.Copy)
                    ins.then_inc(mlp_sbuf, 1)

            fill(0, 0)
            act.wait_ge(consts_in, 16 * 9)
            act.wait_ge(bias2_ready, 1)

            def step(i, v):
                n = NV * i + v
                if before(n, NU - 1):
                    fill(n + 1, (v + 1) % NV)
                if after(n, 1):
                    read_yd(n - 1)
                    sum_y(n - 1, (v - 1) % 2)
                if isinstance(n, int) and NU - NV <= n < NU - NV + 2:
                    if n == NU - NV:
                        act.wait_ge(weights_in, 16 * 6)
                    mlp(0, n - (NU - NV))
                if after(n, 2):
                    act.wait_ge(prod_ready, n - 1)
                    sum_prod(n - 2, range(GB)).then_inc(stage_summed, 1)

            steps(nc.scalar, step)

            read_yd(NU - 1)
            sum_y(NU - 1, 1)
            act.wait_ge(yd_ready, NU + 1)
            act.activation(U[:, NU, :, :], YD[:, P:2 * P], ACT.Copy).then_inc(yd_read, 1)
            mlp(0, 2)
            act.wait_ge(tail_prod, 1)
            sum_prod(NS - 2, range(QB)).then_inc(tail_act, 1)
            mlp(0, 3)
            mlp(1, 0)
            mlp(1, 1)
            act.wait_ge(tail_prod, 2)
            sum_prod(NS - 1, range(QB)).then_inc(tail_act, 1)
            mlp(1, 2)
            mlp(1, 3)
            for phase in range(4):
                mlp(2, phase)

        @block.vector
        def _(dve):
            chain = [0]

            def link(ins):
                chain[0] += 1
                ins.then_inc(dve_step, 1)
                dve.wait_ge(dve_step, chain[0])

            dve.wait_ge(ids_in, 32)
            link(dve.tensor_scalar(idneg[:], ids_sb[:], 0.0, vocab_sb[:, 0:1], ALU.is_lt, ALU.mult))
            link(dve.tensor_tensor(idf[:], ids_sb[:], idneg[:], ALU.add))
            link(dve.tensor_scalar(idneg[:], idf[:], 0.0, vocab_sb[:, 1:2], ALU.max, ALU.min))
            dve.tensor_scalar(idx[:], idneg[:], vocab_sb[:, 2:3], None, ALU.add)\
                .then_inc(index_ready, 1)
            dve.memset(H[:], 0.0).then_inc(h_cleared, 1)
            link(dve.memset(zeros[:], 0.0))
            link(dve.memset(zl[:, 0, :], 0.0))
            dve.wait_ge(consts_in, 16 * 9)
            dve.tensor_scalar(bias2[:], bias_sb[:, 0:1], 2.0, None, ALU.mult)\
                .then_inc(bias2_ready, 1)

            def spread(dst, src):
                dve.tensor_tensor(dst[:], src.broadcast_to([P, GB, F]),
                                  mask_g_sb[:].rearrange("q (x g) -> q x g", x=1)
                                  .broadcast_to([P, GB, F]), ALU.mult).then_inc(zx_ready, 1)

            def spread_z0(s):
                dve.wait_ge(yd_read, 2 * s + 2)
                dve.tensor_reduce(z_diag[:], relu_d[:, bass.ds(s, 1), :, :], axis=AX.X, op=ALU.add)\
                    .then_inc(z_diag_ready, 1)
                dve.wait_ge(y_summed, s + 1)
                dve.wait_ge(z_diag_ready, s + 1)
                dve.tensor_tensor(z0[:, bass.ds(s * GB, GB)], z_off[:, bass.ds(s * GB, GB)],
                                  z_diag[:], ALU.add).then_inc(z0_ready, 1)
                wait(dve, zb_ready, s)
                dve.wait_ge(z0_ready, s + 1)
                spread(zx[0], z0[:, bass.ds(s * GB, GB)].rearrange("q (b x) -> q b x", x=1))

            def spread_zl(s):
                spread(zx[1], zl[:, bass.ds(s, 1), :].rearrange("q x b -> q b x"))

            def outer(s, b0, b1):
                nb = b1 - b0
                return dve.tensor_tensor(
                    prod[:, b0:b1, :, :],
                    U[:, bass.ds(s, 1), b0:b1, :].rearrange("q x b f -> q b f x")
                    .broadcast_to([P, nb, F, F]),
                    zb[:, b0:b1, :].rearrange("q b (x g) -> q b x g", x=1)
                    .broadcast_to([P, nb, F, F]), ALU.mult)

            def sum_prod(s, samples):
                for b in samples:
                    q = prod[:, b, :, :].rearrange("q f g -> q (f g)")
                    last = dve.scalar_tensor_tensor(
                        out=q, in0=q, scalar=bias_sb[:, 1:2], in1=zeros[:], op0=ALU.add,
                        op1=ALU.max, accum_out=zl[:, s + 1, b:b + 1])
                last.then_inc(tail_dve, 1)

            def spread_all(k, l):
                u0, nu = MLP[k]
                src = z0[:, u0 * GB:(u0 + nu) * GB] if l == 0 else \
                    zl[:, u0 + l:u0 + l + nu, :].rearrange("q s b -> q (s b)")
                dve.tensor_tensor(
                    zj[:, l, u0 * UB:(u0 + nu) * UB].rearrange("q (n j b) -> q n j b", n=nu, j=NT),
                    src.rearrange("q (n x b) -> q n x b", n=nu, x=1).broadcast_to([P, nu, NT, GB]),
                    mask_j_sb[:].rearrange("q (x j y) -> q x j y", x=1, y=1)
                    .broadcast_to([P, nu, NT, GB]), ALU.mult).then_inc(zj_ready, 1)

            def products(v, distances):
                for d in distances:
                    last = multiply(dve, v, d)
                return last

            def step(i, v):
                n = NV * i + v
                dve.wait_ge(xt_ready, n + 1)
                wait(dve, y_ready, 2 * (n - 1))
                if isinstance(n, int) and n == NU - NV:
                    for l in range(3):
                        spread_all(0, l)
                distances = dve_distances(n)
                products(v, distances[:CUT1])
                if after(n, 2):
                    spread_z0(n - 2)
                    wait(dve, stage_summed, n - 2)
                    spread_zl(n - 2)
                products(v, distances[CUT1:CUT2])
                if after(n, 2):
                    dve.wait_ge(zb_ready, n - 1)
                    outer(n - 2, 0, GB).then_inc(prod_ready, 1)
                products(v, distances[CUT2:]).then_inc(dve_products, 1)

            steps(nc.vector, step)

            spread_z0(NU - 2)
            dve.wait_ge(stage_summed, NU - 2)
            spread_zl(NU - 2)
            for l in range(3):
                spread_all(1, l)
            dve.wait_ge(zb_ready, NU - 1)
            outer(NU - 2, 0, GB).then_inc(prod_ready, 1)
            dve.wait_ge(prod_ready, NU - 1)
            sum_prod(NU - 2, range(GB))
            for s in range(NU - 1, NS):
                dve.wait_ge(tail_dve, s - NU + 2)
                wait(dve, tail_act, s - NU + 1)
                spread_zl(s)
                if s < NU:
                    spread_z0(s)
                else:
                    dve.wait_ge(yd_read, 2 * NU + 1)
                dve.wait_ge(zb_ready, s + 1)
                outer(s, 0, QB).then_inc(tail_prod, 1)
                outer(s, QB, GB).then_inc(prod_ready, 1)
                if s == NU:
                    spread_all(2, 0)
                    spread_all(2, 1)
                dve.wait_ge(prod_ready, s + 1)
                sum_prod(s, range(QB, GB))
            dve.wait_ge(tail_dve, 3)
            dve.wait_ge(tail_act, 2)
            spread_all(2, 2)

        @block.tensor
        def _(pe):
            def transpose(n, i, v):
                if not (isinstance(n, int) and n == 0):
                    pe.wait_ge(gathered[v], rows_of(v, i))
                wait(pe, xt_ready, n)
                wait(pe, xx_ready, n)
                for j in range(NT):
                    if isinstance(n, int) and n == 0:
                        pe.wait_ge(first_rows[j], 16)
                    for c in range(EC):
                        last = pe.transpose(T[:, c, j * P:(j + 1) * P],
                                            X[:, v, j, c * P:(c + 1) * P], ident_sb[:])
                last.then_inc(transposed, 1)

            def small(cols, terms):
                terms = [(w, s, c) for w, s in terms for c in range(EC)]
                for k, (w, s, c) in enumerate(terms):
                    for j in range(NT):
                        last = pe.matmul(YD[TR * j:TR * j + TR, cols:cols + P], w[:, c, :],
                                         s[:, c, j * P:(j + 1) * P], start=k == 0,
                                         stop=k == len(terms) - 1)
                return last

            def squares_and_u(n, v):
                pe.wait_ge(xt_ready, n + 1)
                pe.wait_ge(xx_ready, n + 1)
                wait(pe, yd_read, 2 * n)
                small(0, [(w0_sb, XX[:, v % 2, :, :])])
                terms = [(w1a_sb, XT[:, v, :, :])]
                if after(n, 1):
                    terms.append((w2a_sb, XT[:, (v - 1) % NV, :, :]))
                small(P, terms).then_inc(yd_ready, 1)

            def contract(n, parity, banks=range(2)):
                pe.wait_ge(dve_products, n + 1)
                pe.wait_ge(pool_products, n + 1)
                wait(pe, y_summed, n - 1)
                for r in banks:
                    for c in range(EC):
                        for j in range(NT):
                            b = GB * j + QB * r
                            last = pe.matmul(
                                Y[TR * j:TR * j + TR, 2 * parity + r, 0:YC], w0_sb[:, c, :],
                                PR[:, parity, c, b:b + QB, :].rearrange("q b s -> q (b s)"),
                                start=c == 0, stop=c == EC - 1)
                    last.then_inc(y_ready, 1)

            def spread_rows(s, layers):
                pe.wait_ge(zx_ready, 2 * s + len(layers))
                wait(pe, prod_ready, s)
                for k in layers:
                    last = pe.matmul(zb, spread_sb[k][:], zx[k][:],
                                     start=k == layers[0], stop=k == layers[-1])
                last.then_inc(zb_ready, 1)

            def mlp(k, phase, chunks=range(HC2)):
                psum, _ = mlp_psum_tiles(k, phase)
                u0, nu = MLP[k]
                cols = slice(u0 * UB, (u0 + nu) * UB)
                done = PER_MLP * k
                if phase == 0:
                    pe.wait_ge(zj_ready, 3 * k + 3)
                    for l in range(3):
                        last = pe.matmul(psum[0], sel_sb[:, l, :], zj[:, l, cols], start=l == 0,
                                         stop=l == 2)
                    last.then_inc(mlp_psum, 1)
                elif phase == 1:
                    pe.wait_ge(mlp_sbuf, done + 1)
                    for c in range(HC1):
                        pe.matmul(psum[c], w1_sb[:, c * P:(c + 1) * P], H[:, cols], start=True,
                                  stop=True).then_inc(mlp_psum, 1)
                elif phase == 2:
                    for c in chunks:
                        for q in range(HC1):
                            pe.wait_ge(mlp_sbuf, done + 2 + q)
                            last = pe.matmul(psum[c], w2_sb[:, q, c * P:(c + 1) * P],
                                             h1[:, q, cols], start=q == 0, stop=q == HC1 - 1)
                        last.then_inc(mlp_psum, 1)
                else:
                    for c in range(HC2):
                        pe.wait_ge(mlp_sbuf, done + 2 + HC1 + c)
                        last = pe.matmul(psum[0], w3_sb[:, c:c + 1], h2[:, c, cols], start=c == 0,
                                         stop=c == HC2 - 1)
                    last.then_inc(mlp_psum, 1)

            pe.wait_ge(consts_in, 16 * 9)
            transpose(0, 0, 0)
            transpose(1, 0, 1)

            def step(i, v):
                n = NV * i + v
                if isinstance(n, int) and n == 2:
                    spread_rows(0, [0, 1])
                if after(n, 1):
                    contract(n - 1, (v - 1) % 2, [0])
                if after(n, 3):
                    spread_rows(n - 2, [0, 1])
                if after(n, 1):
                    contract(n - 1, (v - 1) % 2, [1])
                if isinstance(n, int) and NU - NV <= n < NU - NV + 2:
                    if n == NU - NV:
                        pe.wait_ge(weights_in, 16 * 6)
                        pe.wait_ge(dense_in, 16)
                    pe.wait_ge(xx_ready, n + 2)
                    mlp(0, n - (NU - NV))
                squares_and_u(n, v)
                if before(n, NU - 2):
                    if isinstance(n, int) and n >= NU - NV:
                        pe.wait_ge(mlp_sbuf, (1, 1 + HC1)[n - (NU - NV)])
                    transpose(n + 2, i + (v + 2) // NV, (v + 2) % NV)

            steps(nc.tensor, step)
            spread_rows(NU - 2, [0, 1])
            contract(NU - 1, 1)
            wait(pe, yd_read, 2 * NU)
            small(P, [(w2a_sb, XT[:, NV - 1, :, :])]).then_inc(yd_ready, 1)
            pe.wait_ge(xx_ready, NU)
            mlp(0, 2, [0])
            spread_rows(NU - 1, [0, 1])
            mlp(0, 2, [1])
            pe.wait_ge(y_summed, NU - 1)
            mlp(0, 3)
            mlp(1, 0)
            mlp(1, 1)
            spread_rows(NU, [1])
            mlp(1, 2)
            mlp(1, 3)
            for phase in range(4):
                mlp(2, phase)


def layout(inputs):
    f32 = np.float32
    a = {k: np.asarray(v) for k, v in inputs.items()}
    p = np.arange(P)
    first = np.concatenate([[0], np.cumsum(VOCAB)[:-1]])
    vocab = np.stack([np.tile(v, GB) for v in (np.array(VOCAB), np.array(VOCAB) - 1, first)],
                     axis=1).astype(f32)

    def halves(low, high):
        w = np.zeros((EC, P, TR), f32)
        for at, l in ((0, low), (F, high)):
            if l is not None:
                w[:, :, at:at + F] = a["L0_rec_Ws"][l].T.reshape(EC, P, F)
        return w.transpose(1, 0, 2)

    row, tile = p % TR, p // TR
    same = tile[:, None] == tile[None, :]
    low = row < F
    sel = np.zeros((P, 3, 80), f32)
    for l, rows in ((0, low), (1, low), (2, ~low)):
        sel[p[rows], l, 32 * l + row[rows] % F] = 1
    bs = a["L0_rec_bs"]
    w1 = np.zeros((P, H1), f32)
    for l in range(4):
        w1[32 * l:32 * l + F] = a["W_top1"][F * l:F * l + F]
    return {
        "table": np.concatenate([a[f"tbl_{f}"] for f in range(F)], axis=0),
        "ids": a["ids"].reshape(B // GB, P).T, "vocab": vocab,
        "ident": np.eye(P, dtype=f32),
        "mask_g": (row[:, None] % F == np.arange(F)).astype(f32),
        "mask_j": (tile[:, None] == np.arange(NT)).astype(f32),
        "spread0": (same & low[:, None] & low[None, :]).astype(f32),
        "spread1": (same & low[:, None] & ~low[None, :]).astype(f32),
        "sel": sel,
        "w0": halves(0, 0), "w1a": halves(1, None), "w2a": halves(None, 2),
        "bias": np.stack([np.tile(np.concatenate([bs[0], bs[0]]), NT),
                          np.tile(np.concatenate([bs[1], bs[2]]), NT)], axis=1),
        "w1": w1, "b1": a["b_top1"].reshape(H1 // P, P).T,
        "w2": a["W_top2"].reshape(H1 // P, P, H2).transpose(1, 0, 2),
        "b2": a["b_top2"].reshape(H2 // P, P).T,
        "w3": a["W_top3"].reshape(H2 // P, P).T,
        "dense": a["dense_ctx"].T,
    }


def kernel(**inputs):
    import concourse.bacc as bacc
    from concourse.bass_utils import run_bass_kernel_spmd

    nc = bacc.Bacc("TRN2", target_bir_lowering=False, num_devices=1)
    arrays, args = {}, {}
    for name, v in layout(inputs).items():
        v = np.ascontiguousarray(v)
        arrays[f"in_{name}"] = v
        args[name] = nc.dram_tensor(f"in_{name}", v.shape, mybir.dt.from_np(v.dtype),
                                    kind="ExternalInput").ap()
    out = nc.dram_tensor("out_0", (1, B), F32, kind="ExternalOutput").ap()
    build(nc, out=out, **args)
    r = run_bass_kernel_spmd(nc, [arrays], core_ids=[0])
    return r.results[0]["out_0"].reshape(B, 1)
```

```python
from contextlib import ExitStack

import numpy as np

import concourse.bass as bass
from concourse import mybir

F32 = mybir.dt.float32
I32 = mybir.dt.int32
ACT = mybir.ActivationFunctionType
ALU = mybir.AluOpType
AX = mybir.AxisListType

B, F, E = 512, 16, 256
P = 128
GB = P // F
NT = 4
TR = P // NT
UB = NT * GB
UC = UB * F
NU = B // UB
NV = 4
EC = E // P
PAIRS = F * (F - 1) // 2
QB = GB // 2
YC = QB * PAIRS
NS = NU + 1
H1, H2 = 512, 256
HC1, HC2 = H1 // P, H2 // P
VOCAB = [1250, 1250, 12500, 1000, 12500, 1250, 12500, 1000, 1250, 1250, 1250, 12500, 12500, 1250,
         12500, 12500]
FIRST_PAIR = {8: 0, 4: 64, 2: 96, 1: 112}
POOL_RECT = (5, 8)
POOL_ENDS = {0: (2, 8), 1: (3, 8), 2: (4, 8), NU - 2: (8, 8), NU - 1: (8, 8)}
ACT_SHARES = [GB, GB - 1, GB, GB - 1]
ACT_SHARE = {NU - 5: 7, NU - 4: 6, NU - 3: 3, NU - 2: 2, NU - 1: 4, NU: 2}
ROWS = 80
MLP = [(0, 8), (8, 5), (13, 3)]
MLP_RESULTS = (1, HC1, HC2, 1)
MLP_ORDER = [(0, 0), (0, 1), (1, 0), (0, 2), (1, 1), (0, 3), (1, 2), (1, 3),
             (2, 0), (2, 1), (2, 2), (2, 3)]


def pool_rect(n):
    return POOL_ENDS.get(n, POOL_RECT) if isinstance(n, int) else POOL_RECT


def dve_rects(n):
    a, b = pool_rect(n)
    left = [(8, a, 8, 0, 8)] if a < 8 else []
    left += [(8, 0, a, b, 8)] if b < 8 else []
    quarter = [(2, 0, 2, 0, 2)]
    return ([(4, 0, 4, 0, 4)], [(1, 0, 1, 0, 1)]) + ((left, quarter) if left else (quarter, []))


def mlp_done(k, phase):
    return sum(MLP_RESULTS[p] for _, p in MLP_ORDER[:MLP_ORDER.index((k, phase))])


def act_share(s, slot=None):
    return ACT_SHARES[slot] if slot is not None else ACT_SHARE.get(s, ACT_SHARES[s % NV])


def dve_sums(s):
    return sum(act_share(k) < GB for k in range(s))


def build(nc, table, ids, vocab, ident, mask_g, mask_j, spread0, spread1, sel, w0, w1a, w2a, w2b, bias,
          w1, b1, w2, b2, w3, dense, out):
    ctx = ExitStack()
    with ctx:
        def sb(name, shape, dt=F32):
            return ctx.enter_context(nc.sbuf_tensor(name, shape, dt))

        def pb(name, shape):
            return ctx.enter_context(nc.psum_tensor(name, shape, F32))

        def sem(name):
            return ctx.enter_context(nc.semaphore(name))

        ids_sb = sb("ids_sb", [P, B // GB], I32)
        vocab_sb = sb("vocab_sb", [P, 3])
        idf = sb("idf", [P, B // GB])
        idneg = sb("idneg", [P, B // GB])
        idx = sb("idx", [P, B // GB], I32)
        X = sb("X", [P, NV, NT, E])
        XT = sb("XT", [P, NV, EC, UC])
        XX = sb("XX", [P, 2, EC, UC])
        PR = sb("PR", [P, 2, EC, UB, PAIRS])
        U = sb("U", [P, NS, GB, F])
        terms0 = sb("terms0", [P, NU, GB, F + 1])
        z0 = sb("z0", [P, NU * GB])
        zl = sb("zl", [P, NS + 1, GB])
        zl_cols = zl[:].rearrange("q s b -> q (s b)")
        zx = [sb(f"zx{k}", [P, GB, F]) for k in range(2)]
        prod = sb("prod", [P, GB, F, F])
        zeros = sb("zeros", [P, F * F])
        ident_sb = sb("ident_sb", [P, P])
        mask_g_sb = sb("mask_g_sb", [P, F])
        mask_j_sb = sb("mask_j_sb", [P, NT])
        spread_sb = [sb(f"spread{k}_sb", [P, P]) for k in range(2)]
        sel_sb = sb("sel_sb", [P, 4, ROWS])
        w0_sb = sb("w0_sb", [P, EC, TR])
        w1a_sb = sb("w1a_sb", [P, EC, TR])
        w2a_sb = sb("w2a_sb", [P, EC, TR])
        w2b_sb = sb("w2b_sb", [P, EC, TR])
        bias_sb = sb("bias_sb", [P, 3])
        bias2 = sb("bias2", [P, 1])
        w1_sb = sb("w1_sb", [P, H1])
        b1_sb = sb("b1_sb", [P, HC1])
        w2_sb = sb("w2_sb", [P, HC1, H2])
        b2_sb = sb("b2_sb", [P, HC2])
        w3_sb = sb("w3_sb", [P, HC2])
        zj = sb("zj", [P, 3, B])
        H = sb("H", [P, B])
        h1 = sb("h1", [P, HC1, B])
        h2 = sb("h2", [P, HC2, B])
        y_sb = sb("y_sb", [1, B])

        T = pb("T", [P, 2, EC, UC])
        Y = pb("Y", [P, 2, 512])
        YD = pb("YD", [P, 512])
        ZB = pb("ZB", [P, 512])
        zb = ZB[:, 0:GB * F].rearrange("q (b g) -> q b g", b=GB)

        mask_g_ps = ZB[:, GB * F:GB * F + F]

        ids_in = sem("ids_in")
        consts_in = sem("consts_in")
        weights_in = sem("weights_in")
        dense_in = sem("dense_in")
        index_ready = sem("index_ready")
        dve_step = sem("dve_step")
        bias2_ready = sem("bias2_ready")
        first_rows = [sem(f"first_rows{g}") for g in range(NT)]
        gathered = [sem(f"gathered{v}") for v in range(NV)]
        half_transposed = sem("half_transposed")
        half_ready = sem("half_ready")
        transposed = sem("transposed")
        xt_ready = sem("xt_ready")
        xx_ready = sem("xx_ready")
        dve_products = sem("dve_products")
        pool_products = sem("pool_products")
        yd_ready = sem("yd_ready")
        yd_read = sem("yd_read")
        y_ready = sem("y_ready")
        y_summed = sem("y_summed")
        mask_ready = sem("mask_ready")
        z0_ready = sem("z0_ready")
        zx_ready = sem("zx_ready")
        zb_ready = sem("zb_ready")
        prod_ready = sem("prod_ready")
        tail_prod = sem("tail_prod")
        act_summed = sem("act_summed")
        dve_summed = sem("dve_summed")
        zj_ready = sem("zj_ready")
        h_cleared = sem("h_cleared")
        mlp_psum = sem("mlp_psum")
        mlp_sbuf = sem("mlp_sbuf")
        stored = sem("stored")

        def wait(eng, s, value):
            if not isinstance(value, int) or value > 0:
                eng.wait_ge(s, value)

        def steps(engine, body):
            for v in range(NV):
                body(0, v)
            with engine.Fori(1, NU // NV - 1) as i:
                for v in range(NV):
                    body(i, v)
            for v in range(NV):
                body(NU // NV - 1, v)

        def mlp_psum_tiles(k, phase):
            w = MLP[k][1] * UB

            def split(tiles, n):
                return [tiles[c * len(tiles) // n][:, c % (n // len(tiles)) * w:
                                                   (c % (n // len(tiles)) + 1) * w]
                        for c in range(n)], True

            if k == 0:
                tiles = [([YD[0:ROWS, 2 * P:2 * P + w]], False),
                         ([YD[:, 2 * P:2 * P + w]] * HC1, False),
                         ([T[:, 1, c, 0:w] for c in range(HC2)], False),
                         ([Y[0:1, 0, 0:w]], False)]
            elif k == 1:
                tiles = [([T[0:ROWS, 0, 0, 0:w]], False), split([T[:, 0, 0, :], T[:, 0, 1, :]], HC1),
                         split([T[:, 1, 0, :]], HC2), ([T[0:1, 0, 0, 0:w]], False)]
            else:
                tiles = [([ZB[0:ROWS, 0:w]], False),
                         ([Y[:, 0, 0:w], Y[:, 1, 0:w], T[:, 0, 0, 0:w], T[:, 0, 1, 0:w]], False),
                         ([T[:, 1, c, 0:w] for c in range(HC2)], False), ([YD[0:1, 0:w]], False)]
            return tiles[phase]

        def samples_of(s):
            return QB if isinstance(s, int) and s == NU else GB

        def stage_bias(s):
            return bias_sb[:, 2:3] if isinstance(s, int) and s == NU else bias_sb[:, 1:2]

        def slot_of(n, v):
            return None if isinstance(n, int) else (v - 2) % NV

        def rows_of(v, i):
            return 16 * NT * (i + 1 - (v == 0))

        def before(n, limit):
            return not isinstance(n, int) or n < limit

        def after(n, limit):
            return not isinstance(n, int) or n >= limit

        block = ctx.enter_context(nc.Block())

        @block.sync
        def _(sp):
            sp.dma_start(ids_sb[:], ids).then_inc(ids_in, 16)
            sp.dma_start(vocab_sb[:], vocab).then_inc(ids_in, 16)
            for tile, src in ((ident_sb, ident), (w0_sb, w0), (w1a_sb, w1a), (w2a_sb, w2a), (w2b_sb, w2b),
                              (bias_sb, bias), (mask_g_sb, mask_g), (mask_j_sb, mask_j),
                              (spread_sb[0], spread0), (spread_sb[1], spread1)):
                sp.dma_start(tile[:], src).then_inc(consts_in, 16)
            for tile, src in ((sel_sb, sel), (w1_sb, w1), (b1_sb, b1), (w2_sb, w2), (b2_sb, b2),
                              (w3_sb, w3)):
                sp.dma_start(tile[:], src).then_inc(weights_in, 16)
            sp.wait_ge(h_cleared, 1)
            sp.dma_start(H[96:96 + F, :], dense).then_inc(dense_in, 16)
            sp.wait_ge(mlp_sbuf, mlp_done(2, 3) + 1)
            sp.dma_start(out, y_sb[:]).then_inc(stored, 16)
            sp.wait_ge(stored, 16)

        HALF = UC // 2
        first_T = [T[:, 0, :, 0:HALF], Y[:, :, 0:HALF]]

        def multiply(eng, out, x0, x1, rect):
            h, f0, f1, g0, g1 = rect
            first = FIRST_PAIR[h]
            out = out[:, :, first:first + F // 2 * h].rearrange("q n (k f g) -> q n k f g", f=h,
                                                                g=h)
            if (f0, f1, g0, g1) == (0, h, 0, h):
                out = out.rearrange("q n k f g -> q n k (f g)")
            else:
                out = out[:, :, 0, f0:f1, g0:g1]
            x0 = x0.rearrange("q (n f x) -> q n f x", f=2 * h, x=1)[:, :, f0:f1, :]
            x1 = x1.rearrange("q (n x g) -> q n x g", g=2 * h, x=1)[:, :, :, h + g0:h + g1]
            shape = [P, x0.shape[1], f1 - f0, g1 - g0]
            return eng.tensor_tensor(out, x0.broadcast_to(shape), x1.broadcast_to(shape), ALU.mult)

        def multiply_unit(eng, v, rect):
            x = XT[:, v, :, :].rearrange("q c n -> q (c n)")
            x0 = x if eng is nc.gpsimd else T[:, v % 2, :, :].rearrange("q c n -> q (c n)")
            return multiply(eng, PR[:, v % 2, :, :, :].rearrange("q c b s -> q (c b) s"), x0, x,
                            rect)

        def multiply_half(half, c, rect):
            return multiply(nc.vector, PR[:, 0, c, half * UB // 2:(half + 1) * UB // 2, :],
                            first_T[half][:, c, :], XT[:, 0, c, half * HALF:(half + 1) * HALF],
                            rect)

        @block.gpsimd
        def _(pool):
            pool.wait_ge(index_ready, 1)

            def gather(n):
                wait(pool, transposed, n - NV + 1)
                wait(pool, gathered[n % NV], rows_of(n % NV, n // NV - 1))
                for g in range(NT):
                    pool.indirect_dma_start(
                        out=X[:, n % NV, g, :], out_offset=None, in_=table,
                        in_offset=bass.IndirectOffsetOnAxis(
                            ap=idx[:, NT * n + g:NT * n + g + 1], axis=0),
                    ).then_inc(gathered[n % NV] if n else first_rows[g], 16)

            gather(0)
            gather(1)
            gather(2)
            for n in range(NU):
                pool.wait_ge(xt_ready, n + 1)
                wait(pool, y_ready, 2 * (n - 1))
                a, b = pool_rect(n)
                multiply_unit(nc.gpsimd, n % NV, (8, 0, a, 0, b)).then_inc(pool_products, 1)
                if 1 <= n < NU - 2:
                    gather(n + 2)

        @block.scalar
        def _(act):
            def fill(n, v):
                act.wait_ge(transposed, n + 1)
                wait(act, dve_products, n - NV + 1)
                wait(act, pool_products, n - NV + 1)
                wait(act, yd_ready, n - NV + 2)
                act.activation(XT[:, v, :, :], T[:, v % 2, :, :], ACT.Copy).then_inc(xt_ready, 1)

            def square(n, v):
                act.wait_ge(xt_ready, n + 1)
                wait(act, yd_ready, n - 1)
                act.activation(XX[:, v % 2, :, :], XT[:, v, :, :], ACT.Square)\
                    .then_inc(xx_ready, 1)

            def read_yd(n):
                act.wait_ge(yd_ready, n + 1)
                act.activation(terms0[:, bass.ds(n, 1), :, 0:F], YD[:, 0:P], ACT.Relu,
                               bias=bias_sb[:, 0:1]).then_inc(yd_read, 1)
                act.activation(U[:, bass.ds(n, 1), :, :], YD[:, P:2 * P], ACT.Copy)\
                    .then_inc(yd_read, 1)

            def sum_y(n):
                for r in range(2):
                    act.wait_ge(y_ready, 2 * n + r + 1)
                    for b in range(QB):
                        y = Y[:, r, b * PAIRS:(b + 1) * PAIRS]
                        last = act.activation(
                            y, y, ACT.Relu, bias=bias2[:], scale=2.0,
                            accum_out=terms0[:, bass.ds(n, 1), r * QB + b, F:F + 1])
                last.then_inc(y_summed, 1)

            def sum_prod(s, slot=None):
                for b in range(act_share(s, slot)):
                    q = prod[:, b, :, :]
                    last = act.activation(q, q, ACT.Relu, bias=stage_bias(s),
                                          accum_out=zl[:, bass.ds(s + 1, 1), b:b + 1])
                last.then_inc(act_summed, 1)

            def mlp(k, phase, chunks=None):
                psum, whole = mlp_psum_tiles(k, phase)
                u0, nu = MLP[k]
                cols = slice(u0 * UB, (u0 + nu) * UB)
                size = MLP_RESULTS[phase]
                for c in chunks or range(size):
                    act.wait_ge(mlp_psum, mlp_done(k, phase) + (size if whole else c + 1))
                    if phase == 0:
                        ins = act.activation(H[0:ROWS, cols], psum[c], ACT.Copy)
                    elif phase == 1:
                        ins = act.activation(h1[:, c, cols], psum[c], ACT.Relu,
                                             bias=b1_sb[:, c:c + 1])
                    elif phase == 2:
                        ins = act.activation(h2[:, c, cols], psum[c], ACT.Relu,
                                             bias=b2_sb[:, c:c + 1])
                    else:
                        ins = act.activation(y_sb[:, cols], psum[c], ACT.Copy)
                    ins.then_inc(mlp_sbuf, 1)

            for h, filled, copied in ((0, half_transposed, half_ready), (1, transposed, xt_ready)):
                act.wait_ge(filled, 1)
                act.activation(XT[:, 0, :, h * HALF:(h + 1) * HALF], first_T[h], ACT.Copy)\
                    .then_inc(copied, 1)
            square(0, 0)
            act.wait_ge(consts_in, 16 * 10)
            act.wait_ge(bias2_ready, 1)

            def step(i, v):
                n = NV * i + v
                if before(n, NU - 1):
                    fill(n + 1, (v + 1) % NV)
                if after(n, 1):
                    read_yd(n - 1)
                if isinstance(n, int) and n == NU - 3:
                    act.wait_ge(weights_in, 16 * 6)
                    mlp(0, 0)
                if isinstance(n, int) and n > NU - 3:
                    mlp(0, 1, [n - (NU - 2)])
                if before(n, NU - 1):
                    square(n + 1, (v + 1) % NV)
                if after(n, 1):
                    sum_y(n - 1)
                if after(n, 2):
                    act.wait_ge(prod_ready, n - 1)
                    sum_prod(n - 2, slot_of(n, v))

            steps(nc.scalar, step)

            read_yd(NU - 1)
            mlp(0, 1, [2])
            sum_y(NU - 1)
            act.wait_ge(yd_ready, NU + 1)
            act.activation(U[:, NU, 0:QB, :], YD[:, P:P + QB * F], ACT.Copy).then_inc(yd_read, 1)
            mlp(0, 1, [3])
            mlp(1, 0)
            act.wait_ge(prod_ready, NU - 1)
            sum_prod(NU - 2)
            mlp(0, 2, [0])
            act.wait_ge(tail_prod, 1)
            sum_prod(NU - 1)
            mlp(0, 2, [1])
            mlp(1, 1)
            mlp(0, 3)
            act.wait_ge(tail_prod, 2)
            sum_prod(NU)
            mlp(1, 2)
            mlp(1, 3)
            for phase in range(4):
                mlp(2, phase)

        @block.vector
        def _(dve):
            chain = [0]

            def link(ins):
                chain[0] += 1
                ins.then_inc(dve_step, 1)
                dve.wait_ge(dve_step, chain[0])

            dve.wait_ge(ids_in, 32)
            link(dve.tensor_scalar(idneg[:], ids_sb[:], 0.0, vocab_sb[:, 0:1], ALU.is_lt, ALU.mult))
            link(dve.tensor_tensor(idf[:], ids_sb[:], idneg[:], ALU.add))
            link(dve.tensor_scalar(idneg[:], idf[:], 0.0, vocab_sb[:, 1:2], ALU.max, ALU.min))
            dve.tensor_scalar(idx[:], idneg[:], vocab_sb[:, 2:3], None, ALU.add)\
                .then_inc(index_ready, 1)
            dve.memset(H[:], 0.0).then_inc(h_cleared, 1)
            link(dve.memset(zeros[:], 0.0))
            link(dve.memset(zl[:, 0, :], 0.0))
            dve.wait_ge(consts_in, 16 * 10)
            dve.tensor_scalar(bias2[:], bias_sb[:, 0:1], 2.0, None, ALU.mult)\
                .then_inc(bias2_ready, 1)

            def spread(dst, src):
                dve.tensor_tensor(dst[:], src.broadcast_to([P, GB, F]),
                                  mask_g_ps.rearrange("q (x g) -> q x g", x=1)
                                  .broadcast_to([P, GB, F]), ALU.mult).then_inc(zx_ready, 1)

            def sum_z0(s):
                dve.wait_ge(yd_read, 2 * s + 2)
                dve.wait_ge(y_summed, s + 1)
                dve.tensor_reduce(z0[:, bass.ds(s * GB, GB)],
                                  terms0[:, bass.ds(s, 1), :, :], axis=AX.X, op=ALU.add)\
                    .then_inc(z0_ready, 1)

            def spread_z0(s):
                wait(dve, zb_ready, s)
                dve.wait_ge(z0_ready, s + 1)
                spread(zx[0], z0[:, bass.ds(s * GB, GB)].rearrange("q (b x) -> q b x", x=1))

            def wait_zl(s, i=None, v=None):
                wait(dve, act_summed, s)
                if isinstance(s, int):
                    wait(dve, dve_summed, dve_sums(s))
                else:
                    first = dve_sums(NV + v - 2)
                    each = sum(share < GB for share in ACT_SHARES)
                    dve.wait_ge(dve_summed, each * i + (first - each))

            def spread_zl(s, i=None, v=None):
                wait_zl(s, i, v)
                spread(zx[1], zl[:, bass.ds(s, 1), :].rearrange("q x b -> q b x"))

            def outer(s, b0, b1):
                nb = b1 - b0
                return dve.tensor_tensor(
                    prod[:, b0:b1, :, :],
                    U[:, bass.ds(s, 1), b0:b1, :].rearrange("q x b f -> q b f x")
                    .broadcast_to([P, nb, F, F]),
                    zb[:, b0:b1, :].rearrange("q b (x g) -> q b x g", x=1)
                    .broadcast_to([P, nb, F, F]), ALU.mult)

            def sum_prod(s, slot=None):
                dve.wait_ge(prod_ready, s + 1)
                for b in range(act_share(s, slot), samples_of(s)):
                    q = prod[:, b, :, :].rearrange("q f g -> q (f g)")
                    last = dve.scalar_tensor_tensor(
                        out=q, in0=q, scalar=stage_bias(s), in1=zeros[:], op0=ALU.add,
                        op1=ALU.max, accum_out=zl_cols[:, bass.ds((s + 1) * GB + b, 1)])
                last.then_inc(dve_summed, 1)

            def spread_all(k, l):
                u0, nu = MLP[k]
                nu -= l == 2 and u0 + nu == NU
                src = z0[:, u0 * GB:(u0 + nu) * GB] if l == 0 else \
                    zl[:, u0 + l:u0 + l + nu, :].rearrange("q s b -> q (s b)")
                dve.tensor_tensor(
                    zj[:, l, u0 * UB:(u0 + nu) * UB].rearrange("q (n j b) -> q n j b", n=nu, j=NT),
                    src.rearrange("q (n x b) -> q n x b", n=nu, x=1).broadcast_to([P, nu, NT, GB]),
                    mask_j_sb[:].rearrange("q (x j y) -> q x j y", x=1, y=1)
                    .broadcast_to([P, nu, NT, GB]), ALU.mult).then_inc(zj_ready, 1)

            def spread_last():
                dve.tensor_tensor(
                    zj[:, 2, (NU - 1) * UB:].rearrange("q (j h b) -> q j h b", j=NT, h=2),
                    zl[:, NS, 0:QB].rearrange("q (x y b) -> q x y b", x=1, y=1)
                    .broadcast_to([P, NT, 2, QB]),
                    mask_j_sb[:].rearrange("q (j x y) -> q j x y", x=1, y=1)
                    .broadcast_to([P, NT, 2, QB]), ALU.mult).then_inc(zj_ready, 1)

            def products(v, rects):
                for rect in rects:
                    last = multiply_unit(nc.vector, v, rect)
                return last

            def step(i, v):
                n = NV * i + v
                if isinstance(n, int) and n == 0:
                    for h, copied in ((0, half_ready), (1, xt_ready)):
                        dve.wait_ge(copied, 1)
                        for c in range(EC):
                            for rect in sum(dve_rects(0), []):
                                last = multiply_half(h, c, rect)
                    last.then_inc(dve_products, 1)
                    return
                dve.wait_ge(xt_ready, n + 1)
                wait(dve, y_ready, 2 * (n - 1))
                if isinstance(n, int) and n == NU - NV:
                    for l in range(3):
                        spread_all(0, l)
                rects = dve_rects(n)
                products(v, rects[0])
                if after(n, 2):
                    sum_z0(n - 2)
                products(v, rects[1])
                if after(n, 2):
                    spread_z0(n - 2)
                    spread_zl(n - 2, i, v)
                last = products(v, rects[2])
                if not rects[3]:
                    last.then_inc(dve_products, 1)
                if after(n, 2):
                    dve.wait_ge(zb_ready, n - 1)
                    outer(n - 2, 0, GB).then_inc(prod_ready, 1)
                if rects[3]:
                    products(v, rects[3]).then_inc(dve_products, 1)
                if after(n, 2) and act_share(n - 2, slot_of(n, v)) < GB:
                    sum_prod(n - 2, slot_of(n, v))

            dve.wait_ge(mask_ready, 1)
            steps(nc.vector, step)

            sum_z0(NU - 2)
            spread_z0(NU - 2)
            spread_zl(NU - 2)
            for l in range(3):
                spread_all(1, l)
            dve.wait_ge(zb_ready, NU - 1)
            outer(NU - 2, 0, GB).then_inc(prod_ready, 1)
            sum_prod(NU - 2)
            for s in range(NU - 1, NS):
                if s < NU:
                    sum_z0(s)
                spread_zl(s)
                if s < NU:
                    spread_z0(s)
                else:
                    dve.wait_ge(yd_read, 2 * NU + 1)
                if s == NU:
                    for l in range(3):
                        spread_all(2, l)
                dve.wait_ge(zb_ready, s + 1)
                outer(s, 0, act_share(s)).then_inc(tail_prod, 1)
                outer(s, act_share(s), samples_of(s)).then_inc(prod_ready, 1)
                sum_prod(s)
            wait_zl(NS)
            spread_last()

        @block.tensor
        def _(pe):
            def transpose(n, i, v):
                pe.wait_ge(gathered[v], rows_of(v, i))
                wait(pe, xt_ready, n - 1)
                wait(pe, dve_products, n - 1)
                for j in range(NT):
                    for c in range(EC):
                        last = pe.transpose(T[:, v % 2, c, j * P:(j + 1) * P],
                                            X[:, v, j, c * P:(c + 1) * P], ident_sb[:])
                last.then_inc(transposed, 1)

            def small(cols, terms):
                terms = [(w, s, c) for w, s in terms for c in range(EC)]
                for k, (w, s, c) in enumerate(terms):
                    for j in range(NT):
                        last = pe.matmul(YD[TR * j:TR * j + TR, cols:cols + P], w[:, c, :],
                                         s[:, c, j * P:(j + 1) * P], start=k == 0,
                                         stop=k == len(terms) - 1)
                return last

            def squares_and_u(n, v):
                pe.wait_ge(xt_ready, n + 1)
                pe.wait_ge(xx_ready, n + 1)
                wait(pe, yd_read, 2 * n)
                if isinstance(n, int) and n == NU - 4:
                    pe.wait_ge(weights_in, 16 * 6)
                    pe.wait_ge(dense_in, 16)
                    mlp(0, 0)
                if isinstance(n, int) and n > NU - 4:
                    pe.wait_ge(mlp_sbuf, n - (NU - 4))
                    mlp(0, 1, [n - (NU - 3)])
                small(0, [(w0_sb, XX[:, v % 2, :, :])])
                terms = [(w1a_sb, XT[:, v, :, :])]
                if after(n, 1):
                    terms.append((w2a_sb, XT[:, (v - 1) % NV, :, :]))
                small(P, terms).then_inc(yd_ready, 1)

            def contract(n, parity, banks=range(2)):
                pe.wait_ge(dve_products, n + 1)
                pe.wait_ge(pool_products, n + 1)
                wait(pe, y_summed, n)
                for r in banks:
                    for c in range(EC):
                        for j in range(NT):
                            b = GB * j + QB * r
                            last = pe.matmul(
                                Y[TR * j:TR * j + TR, r, 0:YC], w0_sb[:, c, :],
                                PR[:, parity, c, b:b + QB, :].rearrange("q b s -> q (b s)"),
                                start=c == 0, stop=c == EC - 1)
                    last.then_inc(y_ready, 1)

            def last_u():
                terms = [(w, c, b) for c in range(EC) for w, b in ((w2b_sb, 0), (w2a_sb, QB))]
                for k, (w, c, b) in enumerate(terms):
                    for j in range(NT):
                        first = j * P + b * F
                        last = pe.matmul(YD[TR * j:TR * j + TR, P:P + QB * F], w[:, c, :],
                                         XT[:, NV - 1, c, first:first + QB * F], start=k == 0,
                                         stop=k == len(terms) - 1)
                last.then_inc(yd_ready, 1)

            def spread_last_rows():
                pe.wait_ge(zx_ready, 2 * NU + 1)
                pe.wait_ge(prod_ready, NU)
                for k in range(2):
                    last = pe.matmul(zb[:, 0:QB, :], spread_sb[k][:],
                                     zx[1][:, QB * k:QB * (k + 1), :], start=k == 0, stop=k == 1)
                last.then_inc(zb_ready, 1)

            def spread_rows(s, layers):
                pe.wait_ge(zx_ready, 2 * s + len(layers))
                wait(pe, prod_ready, s)
                for k in layers:
                    last = pe.matmul(zb, spread_sb[k][:], zx[k][:],
                                     start=k == layers[0], stop=k == layers[-1])
                last.then_inc(zb_ready, 1)

            def mlp(k, phase, chunks=None):
                psum, _ = mlp_psum_tiles(k, phase)
                u0, nu = MLP[k]
                cols = slice(u0 * UB, (u0 + nu) * UB)
                if phase == 0:
                    ends = u0 + nu == NU
                    for l in range(3):
                        pe.wait_ge(zj_ready, 3 * k + l + 1)
                        n = (nu - (ends and l == 2)) * UB
                        last = pe.matmul(psum[0][:, 0:n], sel_sb[:, l, :],
                                         zj[:, l, u0 * UB:u0 * UB + n], start=l == 0,
                                         stop=l == 2 and not ends)
                    if ends:
                        pe.wait_ge(zj_ready, 3 * k + 4)
                        out_h = psum[0][:, (nu - 1) * UB:].rearrange("q (j h b) -> q j h b", j=NT,
                                                                     h=2)
                        in_h = zj[:, 2, (NU - 1) * UB:].rearrange("q (j h b) -> q j h b", j=NT, h=2)
                        for h, k_sel in ((0, 3), (1, 2)):
                            last = pe.matmul(out_h[:, :, h, :], sel_sb[:, k_sel, :],
                                             in_h[:, :, h, :], start=False, stop=h == 1)
                    last.then_inc(mlp_psum, 1)
                elif phase == 1:
                    pe.wait_ge(mlp_sbuf, mlp_done(k, 0) + 1)
                    for c in chunks or range(HC1):
                        pe.matmul(psum[c], w1_sb[:, c * P:(c + 1) * P], H[:, cols], start=True,
                                  stop=True).then_inc(mlp_psum, 1)
                elif phase == 2:
                    for c in chunks or range(HC2):
                        for q in range(HC1):
                            pe.wait_ge(mlp_sbuf, mlp_done(k, 1) + q + 1)
                            last = pe.matmul(psum[c], w2_sb[:, q, c * P:(c + 1) * P],
                                             h1[:, q, cols], start=q == 0, stop=q == HC1 - 1)
                        last.then_inc(mlp_psum, 1)
                else:
                    for c in range(HC2):
                        pe.wait_ge(mlp_sbuf, mlp_done(k, 2) + c + 1)
                        last = pe.matmul(psum[0], w3_sb[:, c:c + 1], h2[:, c, cols], start=c == 0,
                                         stop=c == HC2 - 1)
                    last.then_inc(mlp_psum, 1)

            pe.wait_ge(consts_in, 16 * 10)
            pe.matmul(mask_g_ps, ident_sb[:], mask_g_sb[:], start=True, stop=True)\
                .then_inc(mask_ready, 1)
            for h, filled in enumerate((half_transposed, transposed)):
                for j in range(NT // 2):
                    g = NT // 2 * h + j
                    pe.wait_ge(first_rows[g], 16)
                    for c in range(EC):
                        last = pe.transpose(first_T[h][:, c, j * P:(j + 1) * P],
                                            X[:, 0, g, c * P:(c + 1) * P], ident_sb[:])
                last.then_inc(filled, 1)
            transpose(1, 0, 1)

            def step(i, v):
                n = NV * i + v
                if after(n, 1) and before(n, NU - 1):
                    transpose(n + 1, i + (v + 1) // NV, (v + 1) % NV)
                if isinstance(n, int) and n == 2:
                    spread_rows(0, [0, 1])
                if after(n, 1):
                    contract(n - 1, (v - 1) % 2, [0])
                if after(n, 3):
                    spread_rows(n - 2, [0, 1])
                if after(n, 1):
                    contract(n - 1, (v - 1) % 2, [1])
                squares_and_u(n, v)

            steps(nc.tensor, step)
            contract(NU - 1, 1, [0])
            spread_rows(NU - 2, [0, 1])
            contract(NU - 1, 1, [1])
            wait(pe, yd_read, 2 * NU)
            pe.wait_ge(mlp_sbuf, HC1)
            mlp(0, 1, [3])
            last_u()
            mlp(1, 0)
            mlp(0, 2, [0])
            spread_rows(NU - 1, [0, 1])
            mlp(0, 2, [1])
            mlp(1, 1)
            mlp(0, 3)
            spread_last_rows()
            mlp(1, 2)
            mlp(1, 3)
            pe.wait_ge(prod_ready, NS)
            for phase in range(4):
                mlp(2, phase)


def layout(inputs):
    f32 = np.float32
    a = {k: np.asarray(v) for k, v in inputs.items()}
    p = np.arange(P)
    first = np.concatenate([[0], np.cumsum(VOCAB)[:-1]])
    vocab = np.stack([np.tile(v, GB) for v in (np.array(VOCAB), np.array(VOCAB) - 1, first)],
                     axis=1).astype(f32)

    def halves(low, high):
        w = np.zeros((EC, P, TR), f32)
        for at, l in ((0, low), (F, high)):
            if l is not None:
                w[:, :, at:at + F] = a["L0_rec_Ws"][l].T.reshape(EC, P, F)
        return w.transpose(1, 0, 2)

    row, tile = p % TR, p // TR
    same = tile[:, None] == tile[None, :]
    low = row < F
    sel = np.zeros((P, 4, ROWS), f32)
    for at, l, rows in ((0, 0, low), (1, 1, low), (2, 2, ~low), (3, 2, low)):
        sel[p[rows], at, 32 * l + row[rows] % F] = 1
    bs = a["L0_rec_bs"]
    w1 = np.zeros((P, H1), f32)
    for l in range(4):
        w1[32 * l:32 * l + F] = a["W_top1"][F * l:F * l + F]
    return {
        "table": np.concatenate([a[f"tbl_{f}"] for f in range(F)], axis=0),
        "ids": a["ids"].reshape(B // GB, P).T, "vocab": vocab,
        "ident": np.eye(P, dtype=f32),
        "mask_g": (row[:, None] % F == np.arange(F)).astype(f32),
        "mask_j": (tile[:, None] == np.arange(NT)).astype(f32),
        "spread0": (same & low[:, None] & low[None, :]).astype(f32),
        "spread1": (same & low[:, None] & ~low[None, :]).astype(f32),
        "sel": sel,
        "w0": halves(0, 0), "w1a": halves(1, None), "w2a": halves(None, 2),
        "w2b": halves(2, None),
        "bias": np.stack([np.tile(np.concatenate([bs[l], bs[h]]), NT)
                          for l, h in ((0, 0), (1, 2), (2, 2))], axis=1),
        "w1": w1, "b1": a["b_top1"].reshape(H1 // P, P).T,
        "w2": a["W_top2"].reshape(H1 // P, P, H2).transpose(1, 0, 2),
        "b2": a["b_top2"].reshape(H2 // P, P).T,
        "w3": a["W_top3"].reshape(H2 // P, P).T,
        "dense": a["dense_ctx"].T,
    }


def kernel(**inputs):
    import concourse.bacc as bacc
    from concourse.bass_utils import run_bass_kernel_spmd

    nc = bacc.Bacc("TRN2", target_bir_lowering=False, num_devices=1)
    arrays, args = {}, {}
    for name, v in layout(inputs).items():
        v = np.ascontiguousarray(v)
        arrays[f"in_{name}"] = v
        args[name] = nc.dram_tensor(f"in_{name}", v.shape, mybir.dt.from_np(v.dtype),
                                    kind="ExternalInput").ap()
    out = nc.dram_tensor("out_0", (1, B), F32, kind="ExternalOutput").ap()
    build(nc, out=out, **args)
    r = run_bass_kernel_spmd(nc, [arrays], core_ids=[0])
    return r.results[0]["out_0"].reshape(B, 1)
```
